# Optimizing a Trainium2 kernel written in Bass

```python
import numpy as np
import jax
import jax.numpy as jnp

def _softmax(x, axis=-1):
    return jax.nn.softmax(x, axis=axis)

def _gelu(x):
    return jax.nn.gelu(x, approximate=True)

def _silu(x):
    return jax.nn.silu(x)

def _sigmoid(x):
    return jax.nn.sigmoid(x)

def _layernorm(x, axis=-1, eps=1e-05):
    m = jnp.mean(x, axis=axis, keepdims=True)
    v = jnp.var(x, axis=axis, keepdims=True)
    return (x - m) / jnp.sqrt(v + eps)

def _scatter_add(tgt, idx, src, axis=0):
    return tgt.at[idx].add(src)

def _segment_sum(src, seg, n):
    return jax.ops.segment_sum(src, seg, n)
kernel_name = 'mk_hybrid_d1_jaxref_r4_1c4de5'

def setup_inputs(seed: int=0):
    np.random.seed(seed)
    _w = jnp.asarray

    def _L0_attn_a_setup():
        import jax, jax.numpy as jnp
        import numpy as np
        import math
        D_MODEL = 512
        NUM_HEAD = 16
        HEAD_DIM = D_MODEL // NUM_HEAD

        def _trunc_normal(key, shape, std):
            return jax.random.truncated_normal(key, -3.0, 3.0, shape, dtype=jnp.float32) * std
        key = jax.random.key(seed)
        kx, kp, ko = jax.random.split(key, 3)
        b, s = (4, 512)
        x = jax.random.normal(kx, (b, s, D_MODEL), dtype=jnp.float32)
        sigma_p = math.sqrt(2.0 / (D_MODEL + 3 * D_MODEL))
        w_project = _trunc_normal(kp, (3 * D_MODEL, D_MODEL), sigma_p)
        sigma_o = math.sqrt(2.0 / (D_MODEL + D_MODEL))
        w_out = _trunc_normal(ko, (D_MODEL, D_MODEL), sigma_o)
        return {'x': x, 'w_project': w_project, 'w_out': w_out}
    _L0_attn_a_in = _L0_attn_a_setup()

    def _L0_attn_b_setup():
        import jax, jax.numpy as jnp
        import numpy as np
        B, T, C_EMBD, C_ATT = (16, 256, 512, 512)

        def wkv(time_decay, time_first, k, v):
            w = -jnp.exp(time_decay)
            u = time_first
            Bn, Tn, Cn = k.shape

            def step(carry, kv_t):
                aa, bb, pp = carry
                kt, vt = kv_t
                ww = u + kt
                p = jnp.maximum(pp, ww)
                e1 = jnp.exp(pp - p)
                e2 = jnp.exp(ww - p)
                y = (e1 * aa + e2 * vt) / (e1 * bb + e2)
                ww2 = pp + w
                p2 = jnp.maximum(ww2, kt)
                e1b = jnp.exp(ww2 - p2)
                e2b = jnp.exp(kt - p2)
                new = (e1b * aa + e2b * vt, e1b * bb + e2b, p2)
                return (new, y)
            init = (jnp.zeros((Bn, Cn), k.dtype), jnp.zeros((Bn, Cn), k.dtype), jnp.full((Bn, Cn), -1e+38, k.dtype))
            kT = jnp.swapaxes(k, 0, 1)
            vT = jnp.swapaxes(v, 0, 1)
            _, ys = jax.lax.scan(step, init, (kT, vT))
            return jnp.swapaxes(ys, 0, 1)
        key = jax.random.key(seed)
        ks = jax.random.split(key, 10)
        xav = np.sqrt(2.0 / (C_EMBD + C_ATT))
        inp = {'x': jax.random.normal(ks[0], (B, T, C_EMBD), jnp.float32), 'time_decay': jax.random.normal(ks[1], (C_ATT,), jnp.float32) * 0.02, 'time_first': jax.random.normal(ks[2], (C_ATT,), jnp.float32) * 0.02, 'time_mix_k': jax.random.normal(ks[3], (1, 1, C_EMBD), jnp.float32) * 0.02, 'time_mix_v': jax.random.normal(ks[4], (1, 1, C_EMBD), jnp.float32) * 0.02, 'time_mix_r': jax.random.normal(ks[5], (1, 1, C_EMBD), jnp.float32) * 0.02, 'key_w': jax.random.normal(ks[6], (C_ATT, C_EMBD), jnp.float32) * xav, 'value_w': jax.random.normal(ks[7], (C_ATT, C_EMBD), jnp.float32) * xav, 'receptance_w': jax.random.normal(ks[8], (C_ATT, C_EMBD), jnp.float32) * xav, 'output_w': jax.random.normal(ks[9], (C_EMBD, C_ATT), jnp.float32) * xav}
        return inp
    _L0_attn_b_in = _L0_attn_b_setup()

    def _L0_ffn_setup():
        import jax, jax.numpy as jnp
        import numpy as np
        NUM_EXPERTS = 32
        TOP_K = 6
        N_GROUPS = 4
        N_LIMITED_GROUPS = 2
        key = jax.random.key(seed)
        ks = jax.random.split(key, 8)
        H, M = (512, 352)
        SH = 2 * M
        s = 0.02
        return {'hidden_states': jax.random.normal(ks[0], (4, 512, H), jnp.float32), 'gate_w': jax.random.normal(ks[1], (H, NUM_EXPERTS), jnp.float32) * s, 'w_gate': jax.random.normal(ks[2], (NUM_EXPERTS, H, M), jnp.float32) * s, 'w_up': jax.random.normal(ks[3], (NUM_EXPERTS, H, M), jnp.float32) * s, 'w_down': jax.random.normal(ks[4], (NUM_EXPERTS, M, H), jnp.float32) * s, 'sw_gate': jax.random.normal(ks[5], (H, SH), jnp.float32) * s, 'sw_up': jax.random.normal(ks[6], (H, SH), jnp.float32) * s, 'sw_down': jax.random.normal(ks[7], (SH, H), jnp.float32) * s}
    _L0_ffn_in = _L0_ffn_setup()
    _d = {'L0_attn_a_x': _L0_attn_a_in['x'], 'L0_attn_a_w_project': _L0_attn_a_in['w_project'], 'L0_attn_a_w_out': _L0_attn_a_in['w_out'], 'L0_attn_b_time_decay': _L0_attn_b_in['time_decay'], 'L0_attn_b_time_first': _L0_attn_b_in['time_first'], 'L0_attn_b_time_mix_k': _L0_attn_b_in['time_mix_k'], 'L0_attn_b_time_mix_v': _L0_attn_b_in['time_mix_v'], 'L0_attn_b_time_mix_r': _L0_attn_b_in['time_mix_r'], 'L0_attn_b_key_w': _L0_attn_b_in['key_w'], 'L0_attn_b_value_w': _L0_attn_b_in['value_w'], 'L0_attn_b_receptance_w': _L0_attn_b_in['receptance_w'], 'L0_attn_b_output_w': _L0_attn_b_in['output_w'], 'L0_ffn_gate_w': _L0_ffn_in['gate_w'], 'L0_ffn_w_gate': _L0_ffn_in['w_gate'], 'L0_ffn_w_up': _L0_ffn_in['w_up'], 'L0_ffn_w_down': _L0_ffn_in['w_down'], 'L0_ffn_sw_gate': _L0_ffn_in['sw_gate'], 'L0_ffn_sw_up': _L0_ffn_in['sw_up'], 'L0_ffn_sw_down': _L0_ffn_in['sw_down']}
    _x0 = _d['L0_attn_a_x']
    _d['L0_attn_a_x'] = jax.random.normal(jax.random.fold_in(jax.random.key(seed), 1), (1, 2048, 512), dtype=_x0.dtype)
    del _x0
    return _d

def reference(L0_attn_a_x, L0_attn_a_w_project, L0_attn_a_w_out, L0_attn_b_time_decay, L0_attn_b_time_first, L0_attn_b_time_mix_k, L0_attn_b_time_mix_v, L0_attn_b_time_mix_r, L0_attn_b_key_w, L0_attn_b_value_w, L0_attn_b_receptance_w, L0_attn_b_output_w, L0_ffn_gate_w, L0_ffn_w_gate, L0_ffn_w_up, L0_ffn_w_down, L0_ffn_sw_gate, L0_ffn_sw_up, L0_ffn_sw_down):

    def _L0_attn_a_ref(x, w_project, w_out):
        import jax, jax.numpy as jnp
        import numpy as np
        import math
        D_MODEL = 512
        NUM_HEAD = 16
        HEAD_DIM = D_MODEL // NUM_HEAD

        def _trunc_normal(key, shape, std):
            return jax.random.truncated_normal(key, -3.0, 3.0, shape, dtype=jnp.float32) * std
        b, s, d = x.shape
        qkv = jnp.einsum('bsd,od->bso', x, w_project)
        qkv = qkv.reshape(b, s, 3, NUM_HEAD, HEAD_DIM)
        qkv = jnp.transpose(qkv, (2, 0, 3, 1, 4))
        q, k, v = (qkv[0], qkv[1], qkv[2])
        att = jnp.einsum('bhqd,bhkd->bhqk', q, k) / math.sqrt(HEAD_DIM)
        causal = jnp.triu(jnp.ones((s, s), dtype=bool), k=1)
        att = jnp.where(causal[None, None, :, :], jnp.float32(-1000000000.0), att)
        att = jax.nn.softmax(att, axis=-1)
        out = jnp.einsum('bhqk,bhkd->bhqd', att, v)
        out = jnp.transpose(out, (0, 2, 1, 3)).reshape(b, s, d)
        return jnp.einsum('bsd,od->bso', out, w_out)

    def _L0_attn_b_ref(x, time_decay, time_first, time_mix_k, time_mix_v, time_mix_r, key_w, value_w, receptance_w, output_w):
        import jax, jax.numpy as jnp
        import numpy as np
        B, T, C_EMBD, C_ATT = (16, 256, 512, 512)

        def wkv(time_decay, time_first, k, v):
            w = -jnp.exp(time_decay)
            u = time_first
            Bn, Tn, Cn = k.shape

            def step(carry, kv_t):
                aa, bb, pp = carry
                kt, vt = kv_t
                ww = u + kt
                p = jnp.maximum(pp, ww)
                e1 = jnp.exp(pp - p)
                e2 = jnp.exp(ww - p)
                y = (e1 * aa + e2 * vt) / (e1 * bb + e2)
                ww2 = pp + w
                p2 = jnp.maximum(ww2, kt)
                e1b = jnp.exp(ww2 - p2)
                e2b = jnp.exp(kt - p2)
                new = (e1b * aa + e2b * vt, e1b * bb + e2b, p2)
                return (new, y)
            init = (jnp.zeros((Bn, Cn), k.dtype), jnp.zeros((Bn, Cn), k.dtype), jnp.full((Bn, Cn), -1e+38, k.dtype))
            kT = jnp.swapaxes(k, 0, 1)
            vT = jnp.swapaxes(v, 0, 1)
            _, ys = jax.lax.scan(step, init, (kT, vT))
            return jnp.swapaxes(ys, 0, 1)
        xx = jnp.pad(x, ((0, 0), (1, 0), (0, 0)))[:, :-1]
        xk = x * time_mix_k + xx * (1 - time_mix_k)
        xv = x * time_mix_v + xx * (1 - time_mix_v)
        xr = x * time_mix_r + xx * (1 - time_mix_r)
        k = jnp.einsum('btc,dc->btd', xk, key_w)
        v = jnp.einsum('btc,dc->btd', xv, value_w)
        r = jnp.einsum('btc,dc->btd', xr, receptance_w)
        sr = jax.nn.sigmoid(r)
        rwkv = sr * wkv(time_decay, time_first, k, v)
        return jnp.einsum('btd,cd->btc', rwkv, output_w)

    def _L0_ffn_ref(hidden_states, gate_w, w_gate, w_up, w_down, sw_gate, sw_up, sw_down):
        import jax, jax.numpy as jnp
        import numpy as np
        NUM_EXPERTS = 32
        TOP_K = 6
        N_GROUPS = 4
        N_LIMITED_GROUPS = 2
        B, S, H = hidden_states.shape
        E, K = (NUM_EXPERTS, TOP_K)
        x = hidden_states.reshape(-1, H)
        T = x.shape[0]
        scores = jax.nn.sigmoid(x @ gate_w)
        original_scores = scores
        epg = E // N_GROUPS
        sg = scores.reshape(T, N_GROUPS, epg)
        group_scores = jnp.max(sg, axis=-1)
        _, top_groups = jax.lax.top_k(group_scores, N_LIMITED_GROUPS)
        mask = jnp.ones((T, N_GROUPS), dtype=bool)
        mask = mask.at[jnp.arange(T)[:, None], top_groups].set(False)
        sg = jnp.where(mask[:, :, None], -jnp.inf, sg)
        masked_scores = sg.reshape(T, E)
        _, selected_experts = jax.lax.top_k(masked_scores, K)
        weights = jnp.take_along_axis(original_scores, selected_experts, axis=-1)
        weights = weights / jnp.sum(weights, axis=-1, keepdims=True)
        sel_flat = selected_experts.ravel()
        x_exp = jnp.repeat(x, K, axis=0)
        sort_idx = jnp.argsort(sel_flat)
        xs = x_exp[sort_idx]
        group_sizes = jnp.bincount(sel_flat, length=E).astype(jnp.int32)
        g = jax.lax.ragged_dot(xs, w_gate, group_sizes)
        u = jax.lax.ragged_dot(xs, w_up, group_sizes)
        d = jax.lax.ragged_dot(jax.nn.silu(g) * u, w_down, group_sizes)
        unsort_idx = jnp.argsort(sort_idx)
        out = d[unsort_idx].reshape(T, K, H)
        expert_out = jnp.sum(out * weights[..., None], axis=1)
        shared = jax.nn.silu(x @ sw_gate) * (x @ sw_up) @ sw_down
        return (expert_out + shared).reshape(B, S, H)
    x = L0_attn_a_x
    x = x + _L0_attn_a_ref(_layernorm(x, axis=-1), L0_attn_a_w_project, L0_attn_a_w_out)
    x = x + _L0_ffn_ref(_layernorm(x, axis=-1), L0_ffn_gate_w, L0_ffn_w_gate, L0_ffn_w_up, L0_ffn_w_down, L0_ffn_sw_gate, L0_ffn_sw_up, L0_ffn_sw_down)
    x = x + _L0_attn_b_ref(_layernorm(x, axis=-1), L0_attn_b_time_decay, L0_attn_b_time_first, L0_attn_b_time_mix_k, L0_attn_b_time_mix_v, L0_attn_b_time_mix_r, L0_attn_b_key_w, L0_attn_b_value_w, L0_attn_b_receptance_w, L0_attn_b_output_w)
    x = x + _L0_ffn_ref(_layernorm(x, axis=-1), L0_ffn_gate_w, L0_ffn_w_gate, L0_ffn_w_up, L0_ffn_w_down, L0_ffn_sw_gate, L0_ffn_sw_up, L0_ffn_sw_down)
    return x

_drawn_inputs = setup_inputs


def setup_inputs(seed=0):
    import zlib

    import numpy as np

    out = dict(_drawn_inputs(seed))
    spreads = {}
    factors = {'L0_attn_b_time_decay': 8.0,
     'L0_attn_b_time_first': 23.168,
     'L0_attn_b_time_mix_k': 8.0,
     'L0_attn_b_time_mix_v': 7.621,
     'L0_attn_b_time_mix_r': 8.0}
    for name, (base, spread) in spreads.items():
        noise = np.random.default_rng([zlib.crc32(name.encode()), seed]).standard_normal(out[name].shape)
        drawn = base * np.exp(spread * noise) if base else spread * noise
        out[name] = jnp.asarray(drawn.astype(out[name].dtype))
    for name, factor in factors.items():
        out[name] = (out[name] * factor).astype(out[name].dtype)
    return out
```

```python
from contextlib import ExitStack

import numpy as np
import concourse.bass as bass
from concourse import mybir

F32 = mybir.dt.float32
F32R = mybir.dt.float32r
BF16 = mybir.dt.bfloat16
I32 = mybir.dt.int32
U32 = mybir.dt.uint32
ALU = mybir.AluOpType
ACT = mybir.ActivationFunctionType
AX = mybir.AxisListType

P = 128
T = 2048
D = 512
KD = D // P
NT = T // P
BT = 4
NB = NT // BT
BW = BT * P
NH = 16
HD = D // NH
EPS = 1e-5
MASKED = -1e30
LOWEST = -3e38


class Chain:

    def __init__(self, eng, sem):
        self.eng, self.sem, self.n = eng, sem, 0

    def step(self, instruction):
        instruction.then_inc(self.sem, 1)
        self.n += 1

    def wait(self):
        self.eng.wait_ge(self.sem, self.n)

    def link(self, instruction):
        self.step(instruction)
        self.wait()


class Kernel:

    def __init__(self, nc):
        self.nc, self.sems = nc, []

    def sem(self, name):
        self.sems.append(self.nc.alloc_semaphore(name=name))
        return self.sems[-1]

    def end_stage(self):
        self.nc.clear_and_free_semaphores(self.sems)
        self.sems = []
        self.nc.all_engine_barrier()

    def dram(self, name, shape, dt=F32):
        return self.nc.dram_tensor(name, shape, dt, kind="Internal").ap()


def rows(ap):
    return ap.rearrange("(t p) d -> p t d", p=P)





class Norm:

    def __init__(self, k, name, scope, n_blocks=NB):
        nc = k.nc
        self.stats = scope.enter_context(nc.sbuf_tensor(f"{name}_stats", [P, n_blocks, BT, 6], F32))
        self.mean_var = scope.enter_context(nc.sbuf_tensor(f"{name}_mean_var", [P, n_blocks, BT, 2], F32))
        self.var = scope.enter_context(nc.sbuf_tensor(f"{name}_var", [P, n_blocks, BT], F32))
        self.std = scope.enter_context(nc.sbuf_tensor(f"{name}_std", [P, n_blocks, BT], F32))
        self.r0 = scope.enter_context(nc.sbuf_tensor(f"{name}_r0", [P, n_blocks, BT], F32))
        self.half = scope.enter_context(nc.sbuf_tensor(f"{name}_half", [P, n_blocks, BT], F32))
        self.rstd = scope.enter_context(nc.sbuf_tensor(f"{name}_rstd", [P, n_blocks, BT], F32))
        self.var_ready = k.sem(f"{name}_var_ready")
        self.std_ready = k.sem(f"{name}_std_ready")

    def vector_stats(self, chain, b, x):
        v = chain.eng
        for t in range(BT):
            chain.step(v.bn_stats(self.stats[:, b, t, :], x[:, t, :]))
        chain.wait()
        for t in range(BT):
            chain.step(v.bn_aggr(self.mean_var[:, b, t, :], self.stats[:, b, t, :]))
        chain.wait()
        v.tensor_scalar(self.var[:, b, :], self.mean_var[:, b, :, 1], EPS, None, ALU.add).then_inc(self.var_ready, 1)

    def scalar_root(self, act, b):
        act.wait_ge(self.var_ready, b + 1)
        act.activation(self.std[:, b, :], self.var[:, b, :], ACT.Sqrt).then_inc(self.std_ready, 1)

    def vector_rstd(self, chain, b):
        v = chain.eng
        v.wait_ge(self.std_ready, b + 1)
        chain.link(v.reciprocal(self.r0[:, b, :], self.std[:, b, :]))
        chain.link(v.tensor_tensor(self.half[:, b, :], self.r0[:, b, :], self.r0[:, b, :], ALU.mult))
        chain.link(v.tensor_tensor(self.half[:, b, :], self.half[:, b, :], self.var[:, b, :], ALU.mult))
        chain.link(v.tensor_scalar(self.half[:, b, :], self.half[:, b, :], -0.5, 1.5, ALU.mult, ALU.add))
        chain.link(v.tensor_tensor(self.rstd[:, b, :], self.r0[:, b, :], self.half[:, b, :], ALU.mult))

    def vector_normalize(self, v, b, t, out, x):
        return v.tensor_scalar(out, x, self.mean_var[:, b, t, 0:1], self.rstd[:, b, t:t + 1],
                               ALU.subtract, ALU.mult)


def make_identity(pool, ident, blank_sem, done_sem):
    pool.memset(ident, 0.0).then_inc(blank_sem, 1)
    pool.wait_ge(blank_sem, 1)
    pool.affine_select(out=ident, in_=ident, compare_op=ALU.not_equal, fill=1.0, base=0,
                       pattern=[[-1, P]], channel_multiplier=1).then_inc(done_sem, 1)


def stage_qkv(k, x, wqkv, ident, values, qk_hi, qk_lo):
    nc = k.nc
    with ExitStack() as s:
        def sb(name, shape, dt=F32):
            return s.enter_context(nc.sbuf_tensor(name, shape, dt))
        x_in = sb("a_x", [P, NT, D])
        xn = sb("a_xn", [P, NT, D])
        xT = sb("a_xT", [P, KD, T])
        w = sb("a_w", [P, KD, 3 * D])
        NS = 4
        hi = sb("a_hi", [P, NS, BW], F32R)
        lo = sb("a_lo", [P, NS, BW], F32R)
        norm = Norm(k, "a_norm", s)
        p_turn = s.enter_context(nc.psum_tensor("a_p_turn", [P, 2, BW], F32))
        p_mm = s.enter_context(nc.psum_tensor("a_p_mm", [P, 4, BW], F32))

        x_in_sem = [k.sem(f"a_x_loaded{b}") for b in range(NB)]
        w_loaded = k.sem("a_w_loaded")
        blank = k.sem("a_blank")
        ident_ready = k.sem("a_ident_ready")
        steps = k.sem("a_vector_steps")
        normed = k.sem("a_normed")
        turned = k.sem("a_turned")
        xT_ready = k.sem("a_xT_ready")
        product = k.sem("a_product")
        hi_ready = k.sem("a_hi_ready")
        lo_ready = k.sem("a_lo_ready")
        v_ready = k.sem("a_v_ready")
        stored = [k.sem(f"a_stored{i}") for i in range(NS)]

        NQK = 2 * D // P
        PER = NQK + BT
        x_rows = rows(x)

        with nc.Block() as block:
            @block.sync
            def _(sp):
                for b in range(NB):
                    sp.dma_start(x_in[:, b * BT:(b + 1) * BT, :], x_rows[:, b * BT:(b + 1) * BT, :]).then_inc(x_in_sem[b], 16)
                    if b == 0:
                        sp.dma_start(w[:], wqkv).then_inc(w_loaded, 16)
                for b in range(NB):
                    for c in range(NQK):
                        n = b * NQK + c
                        sp.wait_ge(hi_ready, n + 1)
                        sp.dma_start(qk_hi[c * P:(c + 1) * P, b * BW:(b + 1) * BW], hi[:, n % NS, :].bitcast(F32)).then_inc(stored[n % NS], 16)
                        sp.wait_ge(lo_ready, n + 1)
                        sp.dma_start(qk_lo[c * P:(c + 1) * P, b * BW:(b + 1) * BW], lo[:, n % NS, :].bitcast(F32)).then_inc(stored[n % NS], 16)
                for i in range(NS):
                    sp.wait_ge(stored[i], 32 * (NB * NQK // NS))

            @block.gpsimd
            def _(pool):
                make_identity(pool, ident, blank, ident_ready)

            @block.scalar
            def _(act):
                for b in range(NB):
                    norm.scalar_root(act, b)
                for b in range(NB):
                    for i in range(PER):
                        n = b * PER + i
                        act.wait_ge(product, n + 1)
                        if i < NQK:
                            q = b * NQK + i
                            if q >= NS:
                                act.wait_ge(stored[q % NS], 32 * (q // NS))
                            act.activation(hi[:, q % NS, :], p_mm[:, n % 4, :], ACT.Copy).then_inc(hi_ready, 1)
                        else:
                            t = b * BT + i - NQK
                            act.activation(values[:, t, :], p_mm[:, n % 4, :], ACT.Copy).then_inc(v_ready, 1)

            @block.vector
            def _(v):
                chain = Chain(v, steps)
                for b in range(NB):
                    v.wait_ge(x_in_sem[b], 16)
                    norm.vector_stats(chain, b, x_in[:, b * BT:(b + 1) * BT, :])
                    norm.vector_rstd(chain, b)
                    for t in range(BT):
                        norm.vector_normalize(v, b, t, xn[:, b * BT + t, :], x_in[:, b * BT + t, :]).then_inc(normed, 1)
                    for c in range(KD):
                        n = b * KD + c
                        v.wait_ge(turned, n + 1)
                        v.tensor_copy(xT[:, c, b * BW:(b + 1) * BW], p_turn[:, n % 2, :]).then_inc(xT_ready, 1)
                for b in range(NB):
                    for c in range(NQK):
                        q = b * NQK + c
                        v.wait_ge(hi_ready, q + 1)
                        if q >= NS:
                            v.wait_ge(stored[q % NS], 32 * (q // NS))
                        v.tensor_tensor(lo[:, q % NS, :], p_mm[:, (b * PER + c) % 4, :], hi[:, q % NS, :].bitcast(F32), ALU.subtract).then_inc(lo_ready, 1)

            @block.tensor
            def _(pe):
                pe.wait_ge(ident_ready, 1)
                for b in range(NB):
                    pe.wait_ge(normed, (b + 1) * BT)
                    for c in range(KD):
                        n = b * KD + c
                        if n >= 2:
                            pe.wait_ge(xT_ready, n - 1)
                        for t in range(BT):
                            m = pe.transpose(p_turn[:, n % 2, t * P:(t + 1) * P], xn[:, b * BT + t, c * P:(c + 1) * P], ident)
                        m.then_inc(turned, 1)
                pe.wait_ge(w_loaded, 16)
                for b in range(NB):
                    pe.wait_ge(xT_ready, (b + 1) * KD)
                    for i in range(PER):
                        n = b * PER + i
                        if n >= 4:
                            f = n - 4
                            fb, fi = f // PER, f % PER
                            if fi < NQK:
                                pe.wait_ge(lo_ready, fb * NQK + fi + 1)
                            else:
                                pe.wait_ge(v_ready, fb * BT + fi - NQK + 1)
                        for c in range(KD):
                            if i < NQK:
                                m = pe.matmul(p_mm[:, n % 4, :], w[:, c, i * P:(i + 1) * P], xT[:, c, b * BW:(b + 1) * BW],
                                              start=(c == 0), stop=(c == KD - 1))
                            else:
                                t = b * BT + i - NQK
                                m = pe.matmul(p_mm[:, n % 4, :], xT[:, c, t * P:(t + 1) * P], w[:, c, 2 * D:3 * D],
                                              start=(c == 0), stop=(c == KD - 1))
                        m.then_inc(product, 1)


def stage_attention(k, ident, values, qk_hi, qk_lo, shift_rows, heads_out):
    nc = k.nc
    SCALE = HD ** -0.5
    NPART = 3 * HD
    NROW = NPART + 2
    HV = HD + 1
    KV = 3 * HD
    UW = 2 * BW
    units = [(t, u) for t in range(NT) for u in range(-(-(t + 1) * P // UW))]
    steps = [(j, kt) for j in range(NB) for kt in range((j + 1) * BT)]
    last_step = [m for m, (j, kt) in enumerate(steps) if kt == (j + 1) * BT - 1]
    NU, NSTEP = len(units), len(steps)
    NPROB, NCOL, NROWB = 4, 2, 2
    assert NSTEP % NPROB == 0 and NSTEP % NCOL == 0 and NU % NROWB == 0
    FIRST, SPARE = 6, 6
    unit_at = [FIRST + n * (NSTEP - FIRST - SPARE) // NU for n in range(NU)]
    units_of = lambda m: [n for n in range(NU) if unit_at[n] == m]
    turn_at = {last_step[j] + 3: j for j in range(NB - 1)}

    with ExitStack() as s:
        def sb(name, shape, dt=F32):
            return s.enter_context(nc.sbuf_tensor(name, shape, dt))
        q_stack = [sb(f"b_q_stack{i}", [P, T], F32R) for i in range(2)]
        k_stack = [sb(f"b_k_stack{i}", [P, T], F32R) for i in range(2)]
        v_head = [sb(f"b_v_head{i}", [P, NT, HV]) for i in range(2)]
        probs = sb("b_probs", [P, NPROB, BW])
        mask = sb("b_mask", [P, P], BF16)
        mask_t = sb("b_mask_t", [P, P], BF16)
        ident_b = sb("b_ident", [P, P], BF16)
        zeros_b = sb("b_zeros", [P, P], BF16)
        part_max = sb("b_part_max", [P, NT, 2])
        neg_max = sb("b_neg_max", [P, NT])
        shift = sb("b_shift", [P, 2, NT])
        shift_t = sb("b_shift_t", [2 * NT, P])
        out_t = sb("b_out_t", [KV, 2, BW])
        recip = sb("b_recip", [P, BT, 1])
        p_rows = s.enter_context(nc.psum_tensor("b_p_rows", [P, NROWB, UW], F32))
        p_cols = s.enter_context(nc.psum_tensor("b_p_cols", [P, NCOL, BW], F32))
        p_out = s.enter_context(nc.psum_tensor("b_p_out", [P, BW], F32))
        p_turn = s.enter_context(nc.psum_tensor("b_p_turn", [P, BW], F32))
        turned_out = p_turn[:, 0:BT * KV].rearrange("p (t c) -> p t c", t=BT)
        turned_shift = p_turn[0:2 * NT, BT * KV:BT * KV + P]

        blank = k.sem("b_blank")
        const = k.sem("b_const_ready")
        loaded = [k.sem(f"b_stack_loaded{i}") for i in range(2)]
        v_head_ready = k.sem("b_v_head_ready")
        rows_ready = k.sem("b_rows_ready")
        rows_free = k.sem("b_rows_free")
        chain_max = k.sem("b_max_steps")
        shift_ready = k.sem("b_shift_ready")
        shift_turned = k.sem("b_shift_turned")
        shift_copied = k.sem("b_shift_copied")
        shift_stored = k.sem("b_shift_stored")
        shift_loaded = k.sem("b_shift_loaded")
        cols_ready = k.sem("b_cols_ready")
        probs_ready = k.sem("b_probs_ready")
        probs_free = k.sem("b_probs_free")
        out_free = k.sem("b_out_free")
        out_turned = k.sem("b_out_turned")
        turned_free = k.sem("b_turned_free")
        recip_ready = k.sem("b_recip_ready")
        LOADED = 6 * 16

        with nc.Block() as block:
            @block.gpsimd
            def _(pool):
                chain = Chain(pool, blank)
                for i in range(2):
                    chain.link(pool.memset(k_stack[i][NPART:P, :].bitcast(F32), 1.0))
                chain.link(pool.memset(out_t[:], 0.0))
                chain.link(pool.memset(zeros_b[:], 0.0))
                for i in range(2):
                    pool.memset(v_head[i][:, :, HD:HV], 1.0).then_inc(const, 1)
                pool.memset(part_max[:], LOWEST).then_inc(const, 1)
                pool.affine_select(out=ident_b[:], in_=zeros_b[:], compare_op=ALU.not_equal, fill=1.0,
                                   base=0, pattern=[[-1, P]], channel_multiplier=1).then_inc(const, 1)
                pool.affine_select(out=mask[:], in_=zeros_b[:], compare_op=ALU.is_ge, fill=MASKED,
                                   base=0, pattern=[[-1, P]], channel_multiplier=1).then_inc(const, 1)
                pool.affine_select(out=mask_t[:], in_=zeros_b[:], compare_op=ALU.is_ge, fill=MASKED,
                                   base=0, pattern=[[1, P]], channel_multiplier=-1).then_inc(const, 1)
            N_CONST = 6

            @block.sync
            def _(sp):
                def load_stacks(head, i):
                    for part, (q, kk) in enumerate(((qk_hi, qk_hi), (qk_hi, qk_lo), (qk_lo, qk_hi))):
                        dst = slice(part * HD, (part + 1) * HD)
                        sp.dma_start(q_stack[i][dst, :].bitcast(F32), q[bass.ds(head * HD, HD), :]).then_inc(loaded[i], 16)
                        sp.dma_start(k_stack[i][dst, :].bitcast(F32), kk[bass.ds(head * HD + D, HD), :]).then_inc(loaded[i], 16)

                def move_shift(n, i):
                    sp.wait_ge(shift_copied, n + 1)
                    sp.dma_start(shift_rows.rearrange("a (t c) -> (a t) c", c=P), shift_t[:]).then_inc(shift_stored, 16)
                    sp.wait_ge(shift_stored, (n + 1) * 16)
                    sp.dma_start(q_stack[i][NPART:NROW, :].bitcast(F32), shift_rows).then_inc(shift_loaded, 16)
                    sp.wait_ge(shift_loaded, (n + 1) * 16)

                load_stacks(0, 0)
                load_stacks(1, 1)
                move_shift(0, 0)
                with sp.Fori(0, NH // 2) as r:
                    for i in range(2):
                        n = r * 2 + i
                        move_shift(n + 1, 1 - i)
                        sp.wait_ge(probs_free, (n + 1) * NSTEP + NPROB)
                        load_stacks((n + 2) % NH, i)
                for i in range(2):
                    sp.wait_ge(loaded[i], (NH // 2 + 1) * LOADED)

            @block.scalar
            def _(act):
                act.wait_ge(const, N_CONST)

                def take_values(n, i):
                    act.activation(v_head[i][:, :, 0:HD], values[:, :, bass.ds((n % NH) * HD, HD)], ACT.Copy).then_inc(v_head_ready, 1)

                def copy_shift(n):
                    act.wait_ge(shift_turned, n + 1)
                    act.activation(shift_t[:], turned_shift, ACT.Copy).then_inc(shift_copied, 1)

                act.sem_inc(out_free, 1)
                take_values(0, 0)
                copy_shift(0)
                with act.Fori(0, NH // 2) as r:
                    for i in range(2):
                        n = r * 2 + i
                        for m, (j, kt) in enumerate(steps):
                            w = BW - max(kt - j * BT, 0) * P
                            act.wait_ge(cols_ready, n * NSTEP + m + 1)
                            act.wait_ge(probs_free, n * NSTEP + m + 1)
                            act.activation(probs[:, m % NPROB, 0:w], p_cols[:, m % NCOL, 0:w], ACT.Exp,
                                           scale=SCALE).then_inc(probs_ready, 1)
                            if m == NPROB - 1:
                                take_values(n + 1, 1 - i)
                            if m - 1 in last_step:
                                jj = last_step.index(m - 1)
                                act.wait_ge(probs_free, n * NSTEP + m + NPROB)
                                act.activation(out_t[0:HV, jj % 2, :], p_out[0:HV, :], ACT.Copy).then_inc(out_free, 1)
                        act.wait_ge(probs_free, (n + 1) * NSTEP + NPROB)
                        act.activation(out_t[0:HV, (NB - 1) % 2, :], p_out[0:HV, :], ACT.Copy).then_inc(out_free, 1)
                        copy_shift(n + 1)

            @block.vector
            def _(v):
                v.wait_ge(const, N_CONST)

                def reduce_unit(n, u):
                    t, half = units[u]
                    w = min((t + 1) * P - half * UW, UW)
                    v.wait_ge(rows_ready, n * NU + u + 1)
                    v.tensor_reduce(part_max[:, t, half:half + 1], p_rows[:, u % NROWB, 0:w], AX.X, ALU.max).then_inc(rows_free, 1)

                def head_shift(n):
                    v.wait_ge(rows_free, (n + 1) * NU + NROWB)
                    v.tensor_reduce(neg_max[:], part_max[:], AX.X, ALU.max, negate=True).then_inc(chain_max, 1)
                    v.wait_ge(chain_max, n * 2 + 1)
                    v.tensor_copy(shift[:, 0, :].bitcast(F32R), neg_max[:]).then_inc(chain_max, 1)
                    v.wait_ge(chain_max, n * 2 + 2)
                    v.tensor_tensor(shift[:, 1, :], neg_max[:], shift[:, 0, :], ALU.subtract).then_inc(shift_ready, 1)

                def head_out(n, j):
                    v.wait_ge(out_turned, n * NB + j + 1)
                    v.reciprocal(recip[:], turned_out[:, :, HD:HV]).then_inc(recip_ready, 1)
                    v.wait_ge(recip_ready, n * NB + j + 1)
                    v.tensor_tensor(heads_out[:, j * BT:(j + 1) * BT, bass.ds(n * HD, HD)], turned_out[:, :, 0:HD],
                                    recip[:].to_broadcast([P, BT, HD]), ALU.mult).then_inc(turned_free, 1)

                v.sem_inc(rows_free, NROWB)
                v.sem_inc(turned_free, 1)
                for u in range(NU):
                    reduce_unit(0, u)
                head_shift(0)
                with v.Fori(0, NH // 2) as r:
                    for i in range(2):
                        n = r * 2 + i
                        for m in range(NSTEP):
                            for u in units_of(m):
                                reduce_unit(n + 1, u)
                            if m in turn_at:
                                head_out(n, turn_at[m])
                        head_shift(n + 1)
                        head_out(n, NB - 1)

            @block.tensor
            def _(pe):
                pe.wait_ge(const, N_CONST)
                pe.sem_inc(probs_free, NPROB)

                def rows_unit(n, i, u):
                    t, half = units[u]
                    w = min((t + 1) * P - half * UW, UW)
                    pe.wait_ge(rows_free, n * NU + u + 1)
                    for c in range(0, w, BW):
                        cw = min(BW, w - c)
                        diagonal = half * UW + c + cw == (t + 1) * P
                        mm = pe.matmul(p_rows[:, u % NROWB, c:c + cw], q_stack[i][0:NPART, t * P:(t + 1) * P],
                                       k_stack[i][0:NPART, half * UW + c:half * UW + c + cw], start=True, stop=not diagonal)
                        if diagonal:
                            mm = pe.matmul(p_rows[:, u % NROWB, c + cw - P:c + cw], ident_b[:], mask[:], start=False, stop=True)
                    mm.then_inc(rows_ready, 1)

                def turn_shift(n):
                    pe.wait_ge(shift_ready, n + 1)
                    pe.wait_ge(turned_free, n * NB if not isinstance(n, int) else 1)
                    pe.transpose(turned_shift, shift[:].rearrange("p a t -> p (a t)"), ident).then_inc(shift_turned, 1)

                def scores(n, i, m):
                    j, kt = steps[m]
                    d = max(kt - j * BT, 0) * P
                    mm = pe.matmul(p_cols[:, m % NCOL, 0:BW - d], k_stack[i][0:NROW, kt * P:(kt + 1) * P],
                                   q_stack[i][0:NROW, j * BW + d:(j + 1) * BW], start=True, stop=kt < j * BT)
                    if kt >= j * BT:
                        mm = pe.matmul(p_cols[:, m % NCOL, 0:P], ident_b[:], mask_t[:], start=False, stop=True)
                    mm.then_inc(cols_ready, 1)

                def products(n, i, m):
                    j, kt = steps[m]
                    d = max(kt - j * BT, 0) * P
                    if kt == 0:
                        pe.wait_ge(out_free, n * NB + j + 1)
                    pe.wait_ge(probs_ready, n * NSTEP + m + 1)
                    pe.matmul(p_out[0:HV, d:BW], v_head[i][:, kt, :], probs[:, m % NPROB, 0:BW - d],
                              start=(kt == 0), stop=(m in last_step)).then_inc(probs_free, 1)

                def turn_out(n, j):
                    pe.wait_ge(out_free, n * NB + j + 2)
                    pe.wait_ge(turned_free, n * NB + j + 1)
                    for t in range(BT):
                        mm = pe.transpose(turned_out[:, t, :], out_t[:, j % 2, t * P:(t + 1) * P], ident[0:KV, 0:KV])
                    mm.then_inc(out_turned, 1)

                pe.wait_ge(loaded[0], LOADED)
                for u in range(NU):
                    rows_unit(0, 0, u)
                turn_shift(0)
                with pe.Fori(0, NH // 2) as r:
                    for i in range(2):
                        n = r * 2 + i
                        pe.wait_ge(shift_loaded, (n + 1) * 16)
                        pe.wait_ge(v_head_ready, n + 1)
                        for m in range(NSTEP):
                            scores(n, i, m)
                            if m == FIRST:
                                pe.wait_ge(loaded[1 - i], (r + 1 + i) * LOADED)
                            for u in units_of(m):
                                rows_unit(n + 1, 1 - i, u)
                            if m > 0:
                                products(n, i, m - 1)
                            if m in turn_at:
                                turn_out(n, turn_at[m])
                        products(n, i, NSTEP - 1)
                        turn_shift(n + 1)
                        pe.wait_ge(shift_copied, n + 2)
                        turn_out(n, NB - 1)


def stage_attn_out(k, x, wo, ident, heads, resid):
    nc = k.nc
    with ExitStack() as s:
        def sb(name, shape, dt=F32):
            return s.enter_context(nc.sbuf_tensor(name, shape, dt))
        w = sb("c_w", [P, KD, D])
        heads_t = sb("c_heads_t", [P, 2, KD, P])
        p_turn = s.enter_context(nc.psum_tensor("c_p_turn", [P, 2, KD, P], F32))
        p_mm = s.enter_context(nc.psum_tensor("c_p_mm", [P, 2, D], F32))
        x_loaded, w_loaded = k.sem("c_x_loaded"), k.sem("c_w_loaded")
        turned, turned_copied = k.sem("c_turned"), k.sem("c_turned_copied")
        product, added = k.sem("c_product"), k.sem("c_added")

        with nc.Block() as block:
            @block.sync
            def _(sp):
                sp.dma_start(w[:], wo).then_inc(w_loaded, 16)
                sp.dma_start(resid[:], rows(x)).then_inc(x_loaded, 16)

            @block.scalar
            def _(act):
                for t in range(NT):
                    act.wait_ge(turned, t + 1)
                    if t >= 2:
                        act.wait_ge(product, t - 1)
                    act.activation(heads_t[:, t % 2, :, :], p_turn[:, t % 2, :, :], ACT.Copy).then_inc(turned_copied, 1)

            @block.vector
            def _(v):
                v.wait_ge(x_loaded, 16)
                for t in range(NT):
                    v.wait_ge(product, t + 1)
                    v.tensor_tensor(resid[:, t, :], p_mm[:, t % 2, :], resid[:, t, :], ALU.add).then_inc(added, 1)

            @block.tensor
            def _(pe):
                def turn(t):
                    if t >= 2:
                        pe.wait_ge(turned_copied, t - 1)
                    for c in range(KD):
                        m = pe.transpose(p_turn[:, t % 2, c, :], heads[:, t, c * P:(c + 1) * P], ident)
                    m.then_inc(turned, 1)
                turn(0)
                pe.wait_ge(w_loaded, 16)
                for t in range(NT):
                    if t + 1 < NT:
                        turn(t + 1)
                    pe.wait_ge(turned_copied, t + 1)
                    if t >= 2:
                        pe.wait_ge(added, t - 1)
                    for c in range(KD):
                        m = pe.matmul(p_mm[:, t % 2, :], heads_t[:, t % 2, c, :], w[:, c, :], start=(c == 0), stop=(c == KD - 1))
                    m.then_inc(product, 1)


E = 32
TOPK = 6
GROUPS = 4
GROUPS_KEPT = 2
EPG = E // GROUPS
M = 352
SM = 2 * M
FULL = SM // P
TAIL = SM - FULL * P
MC = -(-M // P)
MTAIL = M - (MC - 1) * P
MAX_TILES = (T * TOPK - E) // P + E
TILES = P
assert MAX_TILES <= TILES and MAX_TILES % 2 == 1
ROWS = T + P
UP = KD * 2 * M
WORDS = UP + MC * D
SLOTS = 3


class Dispatch:

    def __init__(self, k, scope, name):
        def sb(what, shape, dt):
            return scope.enter_context(k.nc.sbuf_tensor(f"{name}_{what}", shape, dt))
        self.row_ids = sb("row_ids", [P, TILES], I32)
        self.row_weights = sb("row_weights", [P, TILES], F32)
        self.tile_expert = sb("tile_expert", [1, TILES], I32)
        self.tile_slot = sb("tile_slot", [1, TILES], I32)
        self.n_turns = sb("n_turns", [1, 1], I32)
        self.release = sb("release", [1, E], I32)


def stage_router(k, name, ident, resid, gate_w, shared_up, shared_down, xn_rows, acc_rows, disp):
    nc = k.nc
    with ExitStack() as s:
        def sb(what, shape, dt=F32):
            return s.enter_context(nc.sbuf_tensor(f"{name}_{what}", shape, dt))
        xn = sb("xn", [P, 2 * BT, D])
        xT = sb("xT", [P, KD, T])
        wg = sb("wg", [P, KD, E])
        wup = sb("wup", [P, KD, 2, SM])
        wdown = sb("wdown", [P, FULL + 1, D])
        zero_row = sb("zero_row", [P, D])
        norm = Norm(k, f"{name}_norm", s)
        NG = 2
        act_gate = sb("act_gate", [P, NG, BW])
        up = sb("up", [P, NG, BW])
        hidden = sb("hidden", [P, 2, FULL + 1, BW])
        down = sb("down", [P, 2, D])
        acc = sb("acc", [P, 2, D])
        logits = sb("logits", [P, NT, E])
        group_max = sb("group_max", [P, NT, GROUPS])
        beaten = sb("beaten", [P, NT, GROUPS])
        rank = sb("rank", [P, NT, GROUPS])
        penalty = sb("penalty", [P, NT, GROUPS])
        masked = sb("masked", [P, NT, E])
        top = sb("top", [P, NT, 8])
        top_id = sb("top_id", [P, NT, 8], U32)
        top_idf = sb("top_idf", [P, NT, 8])
        score = sb("score", [P, NT, TOPK])
        score_sum = sb("score_sum", [P, NT])
        weight = sb("weight", [P, NT, TOPK])
        chosen = sb("chosen", [P, TOPK, NT, E])
        taken = sb("taken", [P, NT, E])
        taken_b = sb("taken_b", [P, NT * E], BF16)
        iota_e = sb("iota_e", [P, E])
        iota_p = sb("iota_p", [P, P])
        own_p = sb("own_p", [P, 1])
        token1 = sb("token1", [P, NT])
        before_b = sb("before_b", [P, P], BF16)
        ones_b = sb("ones_b", [P, P], BF16)
        zeros_b = sb("zeros_b", [P, P], BF16)
        base = sb("base", [P, NT, E])
        total = sb("total", [P, E])
        tiles_i = sb("tiles_i", [P, E], I32)
        tiles_f = sb("tiles_f", [P, E])
        ones_e = sb("ones_e", [P, E])
        end = sb("end", [P, E])
        place = sb("place", [P, NT, E])
        picked = sb("picked", [P, NT, E])
        slot_f = sb("slot_f", [P, TOPK, NT])
        slot_i = sb("slot_i", [P, TOPK, NT], I32)
        tile_i = sb("tile_i", [P, TOPK, NT], I32)
        tile_of = sb("tile_of", [P, TOPK, NT])
        row_of = sb("row_of", [P, TOPK, NT])
        NR = 3
        row_hot = sb("row_hot", [P, NR, P])
        tile_hot = sb("tile_hot", [P, NR, 2, TILES])
        table = sb("table", [P, 2, TILES])
        unfilled = sb("unfilled", [P, TILES])
        spare1 = sb("spare1", [P, 1])
        ended = sb("ended", [P, E])
        of_tile = sb("of_tile", [P, 3])
        third_i = sb("third_i", [P, 1], I32)
        third_f = sb("third_f", [P, 1])
        p_mm = s.enter_context(nc.psum_tensor(f"{name}_p_mm", [P, 4, BW], F32))
        p_down = s.enter_context(nc.psum_tensor(f"{name}_p_down", [P, D], F32))
        p_logits = s.enter_context(nc.psum_tensor(f"{name}_p_logits", [P, NT, E], F32))
        p_count = s.enter_context(nc.psum_tensor(f"{name}_p_count", [P, NT, E], F32))
        p_table = s.enter_context(nc.psum_tensor(f"{name}_p_table", [P, 2 * TILES], F32))

        def sem(what):
            return k.sem(f"{name}_{what}")
        w_loaded, gate_loaded = sem("w_loaded"), sem("gate_loaded")
        consts, pool_steps, steps = sem("consts"), sem("pool_steps"), sem("vector_steps")
        normed, turned, xT_ready = sem("normed"), sem("turned"), sem("xT_ready")
        logits_ready, top_ready, exp_ready = sem("logits_ready"), sem("top_ready"), sem("exp_ready")
        taken_ready, before_ready, before_read, total_ready = sem("taken_ready"), sem("before_ready"), sem("before_read"), sem("total_ready")
        hot_ready, hot_used = sem("hot_ready"), sem("hot_used")
        column_ready, row_ready = sem("column_ready"), sem("row_ready")
        product, gate_act, up_copied, hidden_ready = sem("product"), sem("gate_act"), sem("up_copied"), sem("hidden_ready")
        down_ready, down_copied, acc_ready = sem("down_ready"), sem("down_copied"), sem("acc_ready")
        acc_stored = [sem(f"acc_stored{i}") for i in range(2)]
        xn_stored, spare_stored = [sem(f"xn_stored{i}") for i in range(2)], sem("spare_stored")
        NF = FULL + 1
        size_of = lambda f: P if f < FULL else TAIL
        N_CONST = 11
        hots = [(kk, t) for kk in range(TOPK) for t in range(NT)]

        with nc.Block() as block:
            @block.sync
            def _(sp):
                sp.dma_start(wg[:], gate_w).then_inc(gate_loaded, 16)
                sp.dma_start(wup[:], shared_up).then_inc(w_loaded, 16)
                sp.dma_start(wdown[:, 0:FULL, :], shared_down[0:FULL * P, :].rearrange("(c p) d -> p c d", p=P)).then_inc(w_loaded, 16)
                sp.dma_start(wdown[0:TAIL, FULL, :], shared_down[FULL * P:SM, :]).then_inc(w_loaded, 16)
                xn_out, acc_out = rows(xn_rows[0:T, :]), rows(acc_rows[0:T, :])
                sp.wait_ge(consts, N_CONST)
                sp.dma_start(xn_rows[T:ROWS, :], zero_row[:]).then_inc(spare_stored, 16)
                sp.dma_start(acc_rows[T:ROWS, :], zero_row[:]).then_inc(spare_stored, 16)
                for b in range(NB):
                    sp.wait_ge(normed, (b + 1) * BT)
                    sp.dma_start(xn_out[:, b * BT:(b + 1) * BT, :], xn[:, b % 2 * BT:(b % 2 + 1) * BT, :]).then_inc(xn_stored[b % 2], 16)
                for t in range(NT):
                    sp.wait_ge(acc_ready, t + 1)
                    sp.dma_start(acc_out[:, t, :], acc[:, t % 2, :]).then_inc(acc_stored[t % 2], 16)
                for i in range(2):
                    sp.wait_ge(acc_stored[i], 16 * NT // 2)
                    sp.wait_ge(xn_stored[i], 16 * NB // 2)
                sp.wait_ge(spare_stored, 32)

            @block.gpsimd
            def _(pool):
                chain = Chain(pool, pool_steps)
                chain.link(pool.memset(zeros_b[:], 0.0))
                chain.link(pool.memset(ones_b[:], 1.0))
                pool.memset(zero_row[:], 0.0).then_inc(consts, 1)
                pool.memset(ones_e[:], 1.0).then_inc(consts, 1)
                pool.memset(base[:, 0, :], 0.0).then_inc(consts, 1)
                pool.memset(beaten[:], 0.0).then_inc(consts, 1)
                pool.iota(iota_e[:], [[1, E]], base=0, channel_multiplier=0, allow_small_or_imprecise_dtypes=True).then_inc(consts, 1)
                pool.iota(iota_p[:], [[1, P]], base=0, channel_multiplier=0, allow_small_or_imprecise_dtypes=True).then_inc(consts, 1)
                pool.iota(own_p[:], [[1, 1]], base=0, channel_multiplier=1, allow_small_or_imprecise_dtypes=True).then_inc(consts, 1)
                pool.iota(spare1[:], [[1, 1]], base=T + 1, channel_multiplier=1, allow_small_or_imprecise_dtypes=True).then_inc(consts, 1)
                pool.iota(token1[:], [[P, NT]], base=1, channel_multiplier=1, allow_small_or_imprecise_dtypes=True).then_inc(consts, 1)
                pool.memset(rank[:], 0.0).then_inc(consts, 1)
                pool.affine_select(out=before_b[:], in_=zeros_b[:], compare_op=ALU.is_ge, fill=1.0, base=0,
                                   pattern=[[-1, P]], channel_multiplier=1).then_inc(consts, 1)
                for b in range(NB):
                    for f in range(NF):
                        n = b * NF + f
                        z = size_of(f)
                        pool.wait_ge(gate_act, n + 1)
                        pool.wait_ge(up_copied, n + 1)
                        if b >= 2:
                            pool.wait_ge(down_ready, (b - 1) * BT)
                        pool.tensor_tensor(hidden[0:z, b % 2, f, :], act_gate[0:z, n % NG, :], up[0:z, n % NG, :], ALU.mult).then_inc(hidden_ready, 1)
                    for i in range(BT):
                        t = b * BT + i
                        pool.wait_ge(down_copied, t + 1)
                        if t >= 2:
                            pool.wait_ge(acc_stored[t % 2], 16 * (t // 2))
                        pool.tensor_tensor(acc[:, t % 2, :], down[:, t % 2, :], resid[:, t, :], ALU.add).then_inc(acc_ready, 1)

            @block.scalar
            def _(act):
                for b in range(NB):
                    norm.scalar_root(act, b)
                act.wait_ge(top_ready, NT)
                act.activation(score[:], top[:, :, 0:TOPK], ACT.Exp, scale=-1.0).then_inc(exp_ready, 1)
                for b in range(NB):
                    for f in range(NF):
                        n = b * NF + f
                        z = size_of(f)
                        if n >= NG:
                            act.wait_ge(hidden_ready, n - NG + 1)
                        act.wait_ge(product, 2 * n + 1)
                        act.activation(act_gate[0:z, n % NG, :], p_mm[0:z, 2 * (n % 2), :], ACT.Silu).then_inc(gate_act, 1)
                        act.wait_ge(product, 2 * n + 2)
                        act.activation(up[0:z, n % NG, :], p_mm[0:z, 2 * (n % 2) + 1, :], ACT.Copy).then_inc(up_copied, 1)
                    for i in range(BT):
                        t = b * BT + i
                        act.wait_ge(down_ready, t + 1)
                        if t >= 2:
                            act.wait_ge(acc_ready, t - 1)
                        act.activation(down[:, t % 2, :], p_down[:], ACT.Copy).then_inc(down_copied, 1)

            @block.vector
            def _(v):
                chain = Chain(v, steps)
                for b in range(NB):
                    norm.vector_stats(chain, b, resid[:, b * BT:(b + 1) * BT, :])
                    norm.vector_rstd(chain, b)
                    if b >= 2:
                        v.wait_ge(turned, (b - 1) * KD)
                        v.wait_ge(xn_stored[b % 2], 16 * (b // 2))
                    for t in range(BT):
                        norm.vector_normalize(v, b, t, xn[:, b % 2 * BT + t, :], resid[:, b * BT + t, :]).then_inc(normed, 1)
                    for c in range(KD):
                        n = b * KD + c
                        v.wait_ge(turned, n + 1)
                        v.tensor_copy(xT[:, c, b * BW:(b + 1) * BW], p_mm[:, n % 4, :]).then_inc(xT_ready, 1)
                v.wait_ge(consts, N_CONST)
                v.wait_ge(logits_ready, 1)
                chain.link(v.tensor_copy(logits[:], p_logits[:]))
                chain.link(v.tensor_reduce(group_max[:], logits[:].rearrange("p t (g e) -> p t g e", g=GROUPS), AX.X, ALU.max))
                for g in range(GROUPS):
                    rival = group_max[:, :, g:g + 1]
                    if g > 0:
                        chain.step(v.tensor_tensor(beaten[:, :, 0:g], rival.to_broadcast([P, NT, g]), group_max[:, :, 0:g], ALU.is_gt))
                    if g < GROUPS - 1:
                        chain.step(v.tensor_tensor(beaten[:, :, g + 1:GROUPS], rival.to_broadcast([P, NT, GROUPS - 1 - g]),
                                                   group_max[:, :, g + 1:GROUPS], ALU.is_ge))
                    chain.link(v.memset(beaten[:, :, g:g + 1], 0.0))
                    chain.link(v.tensor_tensor(rank[:], rank[:], beaten[:], ALU.add))
                chain.link(v.tensor_scalar(penalty[:], rank[:], GROUPS_KEPT - 0.5, LOWEST, ALU.is_gt, ALU.mult))
                chain.link(v.tensor_tensor(masked[:].rearrange("p t (g e) -> p t g e", g=GROUPS),
                                           logits[:].rearrange("p t (g e) -> p t g e", g=GROUPS),
                                           penalty[:].unsqueeze(3).to_broadcast([P, NT, GROUPS, EPG]), ALU.add))
                for t in range(NT):
                    v.max(top[:, t, :], masked[:, t, :]).then_inc(top_ready, 1)
                v.wait_ge(top_ready, NT)
                for t in range(NT):
                    chain.step(v.max_index(top_id[:, t, :], top[:, t, :], masked[:, t, :]))
                chain.wait()
                chain.link(v.tensor_copy(top_idf[:], top_id[:]))
                for kk in range(TOPK):
                    chain.step(v.tensor_tensor(chosen[:, kk, :, :], iota_e[:].unsqueeze(1).to_broadcast([P, NT, E]),
                                               top_idf[:, :, kk:kk + 1].to_broadcast([P, NT, E]), ALU.is_equal))
                chain.wait()
                chain.link(v.tensor_tensor(taken[:], chosen[:, 0], chosen[:, 1], ALU.add))
                for kk in range(2, TOPK):
                    chain.link(v.tensor_tensor(taken[:], taken[:], chosen[:, kk], ALU.add))
                v.tensor_copy(taken_b[:], taken[:].rearrange("p t e -> p (t e)")).then_inc(taken_ready, 1)
                v.wait_ge(exp_ready, 1)
                chain.link(v.tensor_scalar(score[:], score[:], 1.0, None, ALU.add))
                chain.link(v.reciprocal(score[:], score[:]))
                chain.link(v.tensor_reduce(score_sum[:], score[:], AX.X, ALU.add))
                chain.link(v.reciprocal(score_sum[:], score_sum[:]))
                chain.link(v.tensor_tensor(weight[:], score[:], score_sum[:].unsqueeze(2).to_broadcast([P, NT, TOPK]), ALU.mult))
                v.wait_ge(before_ready, 1)
                v.tensor_copy(place[:], p_count[:]).then_inc(before_read, 1)
                v.wait_ge(total_ready, 1)
                for t in range(1, NT):
                    chain.link(v.tensor_tensor(base[:, t, :], base[:, t - 1, :], p_count[:, t - 1, :], ALU.add))
                chain.link(v.tensor_tensor(total[:], base[:, NT - 1, :], p_count[:, NT - 1, :], ALU.add))
                chain.link(v.tensor_scalar(tiles_i[:], total[:], float(P - 1), None, ALU.add))
                chain.link(v.tensor_scalar(tiles_i[:], tiles_i[:], 7, None, ALU.arith_shift_right))
                chain.link(v.tensor_copy(tiles_f[:], tiles_i[:]))
                chain.link(v.tensor_tensor_scan(end[:], ones_e[:], tiles_f[:], 0.0, ALU.mult, ALU.add))
                chain.link(v.tensor_tensor(total[:], end[:], tiles_f[:], ALU.subtract))
                chain.link(v.tensor_scalar(total[:], total[:], float(P), None, ALU.mult))
                chain.link(v.tensor_tensor(place[:], place[:], base[:], ALU.add))
                chain.link(v.tensor_tensor(place[:], place[:], total[:].unsqueeze(1).to_broadcast([P, NT, E]), ALU.add))
                for kk in range(TOPK):
                    chain.link(v.tensor_tensor(picked[:], chosen[:, kk], place[:], ALU.mult))
                    chain.link(v.tensor_reduce(slot_f[:, kk, :], picked[:], AX.X, ALU.add))
                chain.link(v.tensor_copy(slot_i[:], slot_f[:]))
                chain.link(v.tensor_scalar(tile_i[:], slot_i[:], 7, None, ALU.arith_shift_right))
                chain.link(v.tensor_copy(tile_of[:], tile_i[:]))
                chain.link(v.scalar_tensor_tensor(row_of[:], tile_of[:], -float(P), slot_f[:], ALU.mult, ALU.add))
                for n, (kk, t) in enumerate(hots):
                    r = n % NR
                    if n >= NR:
                        v.wait_ge(hot_used, n - NR + 1)
                    v.tensor_scalar(row_hot[:, r, :], iota_p[:], row_of[:, kk, t:t + 1], None, ALU.is_equal).then_inc(hot_ready, 1)
                    v.tensor_scalar(tile_hot[:, r, 0, :], iota_p[:], tile_of[:, kk, t:t + 1], token1[:, t:t + 1], ALU.is_equal, ALU.mult).then_inc(hot_ready, 1)
                    v.tensor_scalar(tile_hot[:, r, 1, :], iota_p[:], tile_of[:, kk, t:t + 1], weight[:, t, kk:kk + 1], ALU.is_equal, ALU.mult).then_inc(hot_ready, 1)
                v.wait_ge(hot_used, len(hots))
                chain.link(v.tensor_copy(table[:].rearrange("p a t -> p (a t)"), p_table[:]))
                chain.step(v.tensor_copy(disp.row_weights[:], table[:, 1, :]))
                chain.link(v.tensor_scalar(unfilled[:], table[:, 0, :], 0.0, spare1[:], ALU.is_equal, ALU.mult))
                chain.link(v.tensor_tensor(unfilled[:], unfilled[:], table[:, 0, :], ALU.add))
                chain.step(v.tensor_scalar(disp.row_ids[:], unfilled[:], -1.0, None, ALU.add))
                chain.link(v.tensor_scalar(ended[:], end[:], own_p[:], None, ALU.is_le))
                chain.link(v.tensor_reduce(of_tile[:, 0:1], ended[:], AX.X, ALU.add))
                chain.link(v.tensor_scalar(of_tile[:, 0:1], of_tile[:, 0:1], float(E - 1), None, ALU.min))
                chain.link(v.tensor_scalar(third_i[:], of_tile[:, 0:1], 171.0, None, ALU.mult))
                chain.link(v.tensor_scalar(third_i[:], third_i[:], 9, None, ALU.arith_shift_right))
                chain.link(v.tensor_copy(third_f[:], third_i[:]))
                chain.link(v.scalar_tensor_tensor(of_tile[:, 1:2], third_f[:], -float(SLOTS), of_tile[:, 0:1], ALU.mult, ALU.add))
                v.tensor_scalar(of_tile[:, 1:2], of_tile[:, 1:2], float(WORDS), None, ALU.mult).then_inc(column_ready, 1)
                v.wait_ge(row_ready, 1)
                chain.step(v.tensor_copy(disp.tile_expert[:], p_table[0:1, 0:TILES]))
                chain.step(v.tensor_copy(disp.tile_slot[:], p_table[0:1, TILES:2 * TILES]))
                chain.step(v.memset(disp.release[:], 1))
                chain.wait()
                chain.link(v.tensor_copy(disp.n_turns[:], end[0:1, E - 1:E]))
                chain.link(v.tensor_scalar(disp.n_turns[:], disp.n_turns[:], 1, None, ALU.arith_shift_right))
                chain.link(v.tensor_scalar(disp.release[:, SLOTS:E], end[0:1, 0:E - SLOTS], 1.0, None, ALU.add))

            @block.tensor
            def _(pe):
                def shared_block(b):
                    for f in range(NF):
                        n = b * NF + f
                        z = size_of(f)
                        for g in range(2):
                            q = 2 * n + g
                            if q >= 4:
                                pe.wait_ge(gate_act if g == 0 else up_copied, n - 1)
                            for c in range(KD):
                                m = pe.matmul(p_mm[0:z, q % 4, :], wup[:, c, g, f * P:f * P + z], xT[:, c, b * BW:(b + 1) * BW],
                                              start=(c == 0), stop=(c == KD - 1))
                            m.then_inc(product, 1)
                    pe.wait_ge(hidden_ready, (b + 1) * NF)
                    for i in range(BT):
                        t = b * BT + i
                        if t >= 1:
                            pe.wait_ge(down_copied, t)
                        for f in range(NF):
                            z = size_of(f)
                            m = pe.matmul(p_down[:], hidden[0:z, b % 2, f, i * P:(i + 1) * P], wdown[0:z, f, :],
                                          start=(f == 0), stop=(f == NF - 1))
                        m.then_inc(down_ready, 1)

                def tables(first, last):
                    for n in range(first, last):
                        pe.wait_ge(hot_ready, 3 * (n + 1))
                        pe.matmul(p_table[:], row_hot[:, n % NR, :], tile_hot[:, n % NR, :, :].rearrange("p a t -> p (a t)"),
                                  start=(n == 0), stop=(n == len(hots) - 1)).then_inc(hot_used, 1)

                for b in range(NB):
                    pe.wait_ge(normed, (b + 1) * BT)
                    for c in range(KD):
                        n = b * KD + c
                        if n >= 4:
                            pe.wait_ge(xT_ready, n - 3)
                        for t in range(BT):
                            m = pe.transpose(p_mm[:, n % 4, t * P:(t + 1) * P], xn[:, b % 2 * BT + t, c * P:(c + 1) * P], ident)
                        m.then_inc(turned, 1)
                pe.wait_ge(gate_loaded, 16)
                for t in range(NT):
                    pe.wait_ge(xT_ready, (t // BT + 1) * KD)
                    for c in range(KD):
                        m = pe.matmul(p_logits[:, t, :], xT[:, c, t * P:(t + 1) * P], wg[:, c, :], start=(c == 0), stop=(c == KD - 1))
                m.then_inc(logits_ready, 1)
                pe.wait_ge(w_loaded, 48)
                shared_block(0)
                pe.wait_ge(taken_ready, 1)
                count = p_count[:].rearrange("p t e -> p (t e)")
                pe.matmul(count, before_b[:], taken_b[:], start=True, stop=True).then_inc(before_ready, 1)
                pe.wait_ge(before_read, 1)
                pe.matmul(count, ones_b[:], taken_b[:], start=True, stop=True).then_inc(total_ready, 1)
                shared_block(1)
                tables(0, len(hots) // 2)
                shared_block(2)
                tables(len(hots) // 2, len(hots))
                shared_block(3)
                pe.wait_ge(column_ready, 1)
                for i in range(2):
                    m = pe.matmul(p_table[0:1, i * TILES:(i + 1) * TILES], of_tile[:, i:i + 1], ident, start=True, stop=True)
                m.then_inc(row_ready, 1)




def stage_experts(k, name, ident, up_w, down_w, xn_rows, acc_rows, disp):
    nc = k.nc
    TURNS = (MAX_TILES - 1) // 2
    with ExitStack() as s:
        def sb(what, shape, dt=F32):
            return s.enter_context(nc.sbuf_tensor(f"{name}_{what}", shape, dt))
        ring = sb("ring", [P, SLOTS * WORDS])
        rows_in = sb("rows_in", [P, 2, D])
        rows_t = sb("rows_t", [P, 2, KD, P])
        gate = sb("gate", [P, 2, M])
        hidden = sb("hidden", [P, 2, MC * P])
        hidden_t = sb("hidden_t", [P, 2, MC, P])
        y = sb("y", [P, 2, D])
        ids_in = sb("ids_in", [P, 2], I32)
        ids_out = sb("ids_out", [P, 2], I32)
        p_turn = s.enter_context(nc.psum_tensor(f"{name}_p_turn", [P, KD, P], F32))
        p_gate = s.enter_context(nc.psum_tensor(f"{name}_p_gate", [P, 2, BW], F32))
        p_up = s.enter_context(nc.psum_tensor(f"{name}_p_up", [P, 2, BW], F32))
        p_hid = s.enter_context(nc.psum_tensor(f"{name}_p_hid", [P, MC, P], F32))
        p_y = s.enter_context(nc.psum_tensor(f"{name}_p_y", [P, 2, D], F32))

        def sem(what):
            return k.sem(f"{name}_{what}")
        consts, loaded, gathered, turned, rows_ready = sem("consts"), sem("loaded"), [sem(f"gathered{i}") for i in range(2)], sem("turned"), sem("rows_ready")
        products_ready, gate_ready, hidden_ready, hidden_turned, hidden_copied = sem("products_ready"), sem("gate_ready"), sem("hidden_ready"), sem("hidden_turned"), sem("hidden_copied")
        tiles_done, y_ready, y_free, added = sem("tiles_done"), sem("y_ready"), sem("y_free"), sem("added")
        ids_in_ready, ids_out_ready = sem("ids_in_ready"), sem("ids_out_ready")
        slot_free, gather_order, add_order = sem("slot_free"), sem("gather_order"), sem("add_order")
        LOADED = 3 * 16

        def number(eng, ap, most):
            return eng.value_load(ap, min_val=0, max_val=most)

        def turns(eng):
            return number(eng, disp.n_turns[0:1, 0:1], TURNS)

        with nc.Block() as block:
            @block.sync
            def _(sp):
                with sp.Fori(0, E) as e:
                    sp.wait_ge(tiles_done, number(sp, disp.release[0:1, bass.ds(e, 1)], TILES))
                    sp.sem_inc(slot_free, 1)
                    at = (e % SLOTS) * WORDS
                    sp.dma_start(ring[:, bass.ds(at, UP)], up_w[bass.ds(e, 1), :, :].rearrange("e p w -> (e p) w")).then_inc(loaded, 16)
                    sp.dma_start(ring[:, bass.ds(at + UP, (MC - 1) * D)].rearrange("p (c d) -> p c d", d=D),
                                 down_w[bass.ds(e, 1), 0:(MC - 1) * P, :].rearrange("e (c p) d -> p (e c) d", p=P)).then_inc(loaded, 16)
                    sp.dma_start(ring[0:MTAIL, bass.ds(at + UP + (MC - 1) * D, D)],
                                 down_w[bass.ds(e, 1), (MC - 1) * P:M, :].rearrange("e p d -> (e p) d")).then_inc(loaded, 16)
                    sp.wait_ge(loaded, (e + 1) * LOADED)
                    sp.sem_inc(slot_free, 1)

            @block.gpsimd
            def _(pool):
                def gather(t, i):
                    pool.tensor_copy(ids_in[:, i:i + 1], disp.row_ids[:, bass.ds(t, 1)]).then_inc(ids_in_ready, 1)
                    pool.wait_ge(ids_in_ready, t + 1)
                    pool.sem_inc(gather_order, 1)
                    pool.indirect_dma_start(out=rows_in[:, i, :], out_offset=None, in_=xn_rows,
                                            in_offset=bass.IndirectOffsetOnAxis(ap=ids_in[:, i:i + 1].bitcast(U32), axis=0)).then_inc(gathered[i], 16)

                def add(t, i):
                    pool.tensor_copy(ids_out[:, i:i + 1], disp.row_ids[:, bass.ds(t, 1)]).then_inc(ids_out_ready, 1)
                    pool.wait_ge(ids_out_ready, t + 1)
                    pool.wait_ge(y_ready, t + 1)
                    pool.sem_inc(add_order, 1)
                    pool.indirect_dma_start(out=acc_rows, out_offset=bass.IndirectOffsetOnAxis(ap=ids_out[:, i:i + 1].bitcast(U32), axis=0),
                                            in_=y[:, i, :], in_offset=None, compute_op=ALU.add).then_inc(added, 16)
                    pool.wait_ge(added, (t + 1) * 16)
                    pool.sem_inc(y_free, 1)

                pool.memset(hidden[:], 0.0).then_inc(consts, 1)
                pool.sem_inc(y_free, 2)
                gather(0, 0)
                gather(1, 1)
                with pool.Fori(0, TURNS) as r:
                    for i in range(2):
                        t = r * 2 + 1 + i
                        pool.wait_ge(turned, t + 1)
                        gather(t + 1, i)
                        add(t - 1, i)
                add(TURNS * 2, 0)
                pool.wait_ge(gathered[1], 16)

            @block.scalar
            def _(act):
                def copy_rows(t, i):
                    act.wait_ge(turned, t + 1)
                    act.activation(rows_t[:, i, :, :], p_turn[:], ACT.Copy).then_inc(rows_ready, 1)

                def silu(t, i):
                    act.wait_ge(products_ready, 2 * t + 1)
                    act.activation(gate[:, i, :], p_gate[:, i, 0:M], ACT.Silu).then_inc(gate_ready, 1)

                def scale_y(t, i):
                    act.wait_ge(tiles_done, t + 2)
                    act.wait_ge(y_free, t + 1)
                    act.activation(y[:, i, :], p_y[:, i, :], ACT.Copy, scale=disp.row_weights[:, bass.ds(t, 1)]).then_inc(y_ready, 1)

                copy_rows(0, 0)
                silu(0, 0)
                with act.Fori(0, TURNS) as r:
                    for i in range(2):
                        t = r * 2 + 1 + i
                        act.wait_ge(products_ready, 2 * (t - 1) + 2)
                        copy_rows(t, 1 - i)
                        silu(t, 1 - i)
                        scale_y(t - 1, i)
                scale_y(TURNS * 2, 0)

            @block.vector
            def _(v):
                def multiply(t, i):
                    v.wait_ge(gate_ready, t + 1)
                    v.wait_ge(products_ready, 2 * t + 2)
                    v.tensor_tensor(hidden[:, i, 0:M], gate[:, i, :], p_up[:, i, 0:M], ALU.mult).then_inc(hidden_ready, 1)

                def copy_hidden(t, i):
                    v.wait_ge(hidden_turned, t + 1)
                    v.tensor_copy(hidden_t[:, i, :, :], p_hid[:]).then_inc(hidden_copied, 1)

                v.wait_ge(consts, 1)
                multiply(0, 0)
                copy_hidden(0, 0)
                with v.Fori(0, TURNS) as r:
                    for i in range(2):
                        t = r * 2 + 1 + i
                        multiply(t, 1 - i)
                        copy_hidden(t, 1 - i)

            @block.tensor
            def _(pe):
                def turn_rows(t, i, count):
                    pe.wait_ge(gathered[i], count * 16)
                    for c in range(KD):
                        m = pe.transpose(p_turn[:, c, :], rows_in[:, i, c * P:(c + 1) * P], ident)
                    m.then_inc(turned, 1)

                def up(t, i):
                    expert = number(pe, disp.tile_expert[0:1, bass.ds(t, 1)], E - 1)
                    at = number(pe, disp.tile_slot[0:1, bass.ds(t, 1)], (SLOTS - 1) * WORDS)
                    pe.wait_ge(loaded, (expert + 1) * LOADED)
                    pe.wait_ge(rows_ready, t + 1)
                    for g, p_g in enumerate((p_gate, p_up)):
                        for c in range(KD):
                            m = pe.matmul(p_g[:, i, 0:M], rows_t[:, i, c, :], ring[:, bass.ds(at + (c * 2 + g) * M, M)],
                                          start=(c == 0), stop=(c == KD - 1))
                        m.then_inc(products_ready, 1)

                def turn_hidden(t, i):
                    pe.wait_ge(hidden_ready, t + 1)
                    for c in range(MC):
                        m = pe.transpose(p_hid[:, c, :], hidden[:, i, c * P:(c + 1) * P], ident)
                    m.then_inc(hidden_turned, 1)

                def down(t, i):
                    at = number(pe, disp.tile_slot[0:1, bass.ds(t, 1)], (SLOTS - 1) * WORDS) + UP
                    pe.wait_ge(hidden_copied, t + 1)
                    for c in range(MC):
                        z = P if c < MC - 1 else MTAIL
                        m = pe.matmul(p_y[:, i, :], hidden_t[0:z, i, c, :], ring[0:z, bass.ds(at + c * D, D)],
                                      start=(c == 0), stop=(c == MC - 1))
                    m.then_inc(tiles_done, 1)

                pe.sem_inc(tiles_done, 1)
                turn_rows(0, 0, 1)
                up(0, 0)
                turn_hidden(0, 0)
                with pe.Fori(0, TURNS) as r:
                    for i in range(2):
                        t = r * 2 + 1 + i
                        pe.wait_ge(rows_ready, t)
                        turn_rows(t, 1 - i, r + 1 + i)
                        up(t, 1 - i)
                        down(t - 1, i)
                        turn_hidden(t, 1 - i)
                down(TURNS * 2, 0)



NEG = -1e38


def stage_rwkv(k, ident, x_rows, mixes, decay, first, w_kvr, w_out, out_rows):
    nc = k.nc
    K_, V_, R_ = range(3)
    with ExitStack() as s:
        def sb(what, shape, dt=F32):
            return s.enter_context(nc.sbuf_tensor(f"r_{what}", shape, dt))
        xn = sb("xn", [P, BT, D])
        xT = sb("xT", [P, 2, KD, BW + 1])
        NMIX = 2
        mixed = sb("mixed", [P, NMIX, KD, BW])
        wkvr = sb("wkvr", [P, 3, KD, D])
        wo = sb("wo", [P, KD, D])
        mix = sb("mix", [P, 3, KD])
        mix1 = sb("mix1", [P, 3, KD])
        w = sb("w", [P, KD])
        u = sb("u", [P, KD])
        kvr = sb("kvr", [P, 3, 2, KD, BW])
        pp = sb("pp", [P, KD, BW + 1])
        aa = sb("aa", [P, KD, BW + 1])
        bb = sb("bb", [P, KD, BW + 1])
        keep = sb("keep", [P, KD, BW])
        take = sb("take", [P, KD, BW])
        ev = sb("ev", [P, KD, BW])
        peak = sb("peak", [P, KD, BW])
        e1 = sb("e1", [P, KD, BW])
        e2 = sb("e2", [P, KD, BW])
        y = sb("y", [P, KD, BW])
        x_add = sb("x_add", [P, 2, D])
        norm = Norm(k, "r_norm", s)
        p_turn = s.enter_context(nc.psum_tensor("r_p_turn", [P, 2, BW], F32))
        p_mm = s.enter_context(nc.psum_tensor("r_p_mm", [P, 4, BW], F32))
        p_out = s.enter_context(nc.psum_tensor("r_p_out", [P, 2, D], F32))

        def sem(what):
            return k.sem(f"r_{what}")
        x_loaded, vec_loaded, w_loaded, wo_loaded = sem("x_loaded"), sem("vec_loaded"), sem("w_loaded"), sem("wo_loaded")
        steps, w_exp, normed, turned, xT_ready = sem("vector_steps"), sem("w_exp"), sem("normed"), sem("turned"), sem("xT_ready")
        scaled, mixed_ready, product, copied = sem("scaled"), sem("mixed_ready"), sem("product"), sem("copied")
        pp_ready, keep_exponent, peak_ready = sem("pp_ready"), sem("keep_exponent"), sem("peak_ready")
        take_exponent, e_exponents, ev_ready, weights_ready, e_ready = sem("take_exponent"), sem("e_exponents"), sem("ev_ready"), sem("weights_ready"), sem("e_ready")
        scans_done, fraction_ready, y_ready, pool_steps = sem("scans_done"), sem("fraction_ready"), sem("y_ready"), sem("pool_steps")
        out_ready, out_added = sem("out_ready"), sem("out_added")
        x_add_loaded = [sem(f"x_add_loaded{i}") for i in range(2)]
        out_stored = [sem(f"out_stored{i}") for i in range(2)]
        x_tiles, out_tiles = rows(x_rows), rows(out_rows)
        NPROD = 3 * KD

        with nc.Block() as block:
            @block.sync
            def _(sp):
                def load_x(b):
                    sp.dma_start(xn[:], x_tiles[:, b * BT:(b + 1) * BT, :]).then_inc(x_loaded, 16)
                load_x(0)
                sp.dma_start(mix[:], mixes).then_inc(vec_loaded, 16)
                sp.dma_start(w[:], decay).then_inc(vec_loaded, 16)
                sp.dma_start(u[:], first).then_inc(vec_loaded, 16)
                sp.dma_start(wkvr[:], w_kvr).then_inc(w_loaded, 16)
                sp.dma_start(wo[:], w_out).then_inc(wo_loaded, 16)
                for b in range(1, NB):
                    sp.wait_ge(turned, b * KD)
                    load_x(b)
                for t in range(NT):
                    if t >= 2:
                        sp.wait_ge(out_stored[t % 2], 16 * (t // 2))
                    sp.dma_start(x_add[:, t % 2, :], x_tiles[:, t, :]).then_inc(x_add_loaded[t % 2], 16)
                    sp.wait_ge(out_added, t + 1)
                    sp.dma_start(out_tiles[:, t, :], x_add[:, t % 2, :]).then_inc(out_stored[t % 2], 16)
                for i in range(2):
                    sp.wait_ge(out_stored[i], 16 * NT // 2)

            @block.gpsimd
            def _(pool):
                chain = Chain(pool, pool_steps)
                for b in range(NB):
                    kb, vb = kvr[:, K_, b % 2], kvr[:, V_, b % 2]
                    pool.wait_ge(pp_ready, (b + 1) * KD)
                    pool.tensor_tensor(take[:], kb, pp[:, :, 1:BW + 1], ALU.subtract).then_inc(take_exponent, 1)
                    pool.wait_ge(peak_ready, (b + 1) * KD)
                    pool.tensor_tensor(e1[:], pp[:, :, 0:BW], peak[:], ALU.subtract).then_inc(e_exponents, 1)
                    pool.tensor_tensor(e2[:], kb, peak[:], ALU.subtract).then_inc(e_exponents, 1)
                    pool.wait_ge(weights_ready, 2 * (b + 1))
                    pool.wait_ge(copied, b * NPROD + 2 * KD)
                    pool.tensor_tensor(ev[:], take[:], vb, ALU.mult).then_inc(ev_ready, 1)
                    pool.wait_ge(scans_done, (b + 1) * 2 * KD)
                    pool.wait_ge(e_ready, (b + 1) * (KD + 1))
                    chain.step(pool.tensor_tensor(keep[:], e1[:], aa[:, :, 0:BW], ALU.mult))
                    chain.step(pool.tensor_tensor(ev[:], e2[:], vb, ALU.mult))
                    chain.step(pool.tensor_tensor(peak[:], e1[:], bb[:, :, 0:BW], ALU.mult))
                    chain.wait()
                    pool.tensor_tensor(peak[:], peak[:], e2[:], ALU.add).then_inc(fraction_ready, 1)
                    pool.tensor_tensor(keep[:], keep[:], ev[:], ALU.add).then_inc(fraction_ready, 1)

            @block.scalar
            def _(act):
                def scale_mixes(b, j):
                    n = b * 3 + j
                    act.wait_ge(xT_ready, (b + 1) * (KD + 1))
                    if n >= NMIX:
                        act.wait_ge(product, (n - NMIX + 1) * KD)
                    for c in range(KD):
                        act.activation(mixed[:, n % NMIX, c, :], xT[:, b % 2, c, 1:BW + 1], ACT.Copy,
                                       scale=mix[:, j, c:c + 1]).then_inc(scaled, 1)

                def copy_products(b, j):
                    for c in range(KD):
                        n = b * NPROD + j * KD + c
                        act.wait_ge(product, n + 1)
                        if b >= 2 and c == 0:
                            act.wait_ge(y_ready, b - 1)
                        act.activation(kvr[:, j, b % 2, c, :], p_mm[:, n % 4, :], ACT.Exp if j == R_ else ACT.Copy,
                                       scale=-1.0 if j == R_ else 1.0).then_inc(copied, 1)

                def weights(b):
                    act.wait_ge(keep_exponent, (b + 1) * KD)
                    act.activation(keep[:], keep[:], ACT.Exp).then_inc(weights_ready, 1)
                    act.wait_ge(take_exponent, b + 1)
                    act.activation(take[:], take[:], ACT.Exp).then_inc(weights_ready, 1)

                def e_weights(b):
                    act.wait_ge(e_exponents, 2 * (b + 1))
                    act.activation(e1[:], e1[:], ACT.Exp).then_inc(e_ready, 1)
                    for c in range(KD):
                        act.activation(e2[:, c, :], e2[:, c, :], ACT.Exp, bias=u[:, c:c + 1]).then_inc(e_ready, 1)

                norm.scalar_root(act, 0)
                act.wait_ge(vec_loaded, 48)
                act.activation(w[:], w[:], ACT.Exp).then_inc(w_exp, 1)
                scale_mixes(0, K_)
                scale_mixes(0, V_)
                for b in range(NB + 1):
                    if b < NB:
                        copy_products(b, K_)
                        scale_mixes(b, R_)
                    if b + 1 < NB:
                        norm.scalar_root(act, b + 1)
                    if b >= 1:
                        weights(b - 1)
                    if b < NB:
                        copy_products(b, V_)
                        if b + 1 < NB:
                            scale_mixes(b + 1, K_)
                    if b >= 1:
                        e_weights(b - 1)
                    if b < NB:
                        copy_products(b, R_)
                        if b + 1 < NB:
                            scale_mixes(b + 1, V_)

            @block.vector
            def _(v):
                chain = Chain(v, steps)

                def front(b):
                    v.wait_ge(x_loaded, 16 * (b + 1))
                    norm.vector_stats(chain, b, xn[:])
                    norm.vector_rstd(chain, b)
                    for t in range(BT):
                        norm.vector_normalize(v, b, t, xn[:, t, :], xn[:, t, :]).then_inc(normed, 1)
                    if b == 0:
                        v.memset(xT[:, 0, :, 0:1], 0.0).then_inc(xT_ready, 1)
                    else:
                        v.tensor_copy(xT[:, b % 2, :, 0:1], xT[:, (b - 1) % 2, :, BW:BW + 1]).then_inc(xT_ready, 1)
                    for c in range(KD):
                        n = b * KD + c
                        v.wait_ge(turned, n + 1)
                        v.tensor_copy(xT[:, b % 2, c, 1:BW + 1], p_turn[:, n % 2, :]).then_inc(xT_ready, 1)

                def finish_mix(b, j):
                    n = b * 3 + j
                    for c in range(KD):
                        v.wait_ge(scaled, n * KD + c + 1)
                        v.scalar_tensor_tensor(mixed[:, n % NMIX, c, :], xT[:, b % 2, c, 0:BW], mix1[:, j, c:c + 1],
                                               mixed[:, n % NMIX, c, :], ALU.mult, ALU.add).then_inc(mixed_ready, 1)

                def recurrence_1(b):
                    kb = kvr[:, K_, b % 2]
                    if b == 0:
                        chain.step(v.memset(pp[:, :, 0:1], NEG))
                        chain.step(v.memset(aa[:, :, 0:1], 0.0))
                        chain.step(v.memset(bb[:, :, 0:1], 0.0))
                    else:
                        v.wait_ge(fraction_ready, 2 * b)
                        for carry in (pp, aa, bb):
                            chain.step(v.tensor_copy(carry[:, :, 0:1], carry[:, :, BW:BW + 1]))
                    chain.wait()
                    v.wait_ge(copied, b * NPROD + KD)
                    for c in range(KD):
                        v.tensor_tensor_scan(pp[:, c, 1:BW + 1], w[:, c:c + 1].to_broadcast([P, BW]), kb[:, c, :], pp[:, c, 0:1],
                                             ALU.add, ALU.max).then_inc(pp_ready, 1)
                    v.wait_ge(pp_ready, (b + 1) * KD)
                    if b >= 1:
                        v.wait_ge(y_ready, b)
                    for c in range(KD):
                        v.scalar_tensor_tensor(peak[:, c, :], kb[:, c, :], u[:, c:c + 1], pp[:, c, 0:BW], ALU.add, ALU.max).then_inc(peak_ready, 1)
                    for c in range(KD):
                        v.scalar_tensor_tensor(keep[:, c, :], pp[:, c, 0:BW], w[:, c:c + 1], pp[:, c, 1:BW + 1], ALU.add, ALU.subtract).then_inc(keep_exponent, 1)

                def recurrence_2(b):
                    v.wait_ge(weights_ready, 2 * (b + 1))
                    for c in range(KD):
                        v.tensor_tensor_scan(bb[:, c, 1:BW + 1], keep[:, c, :], take[:, c, :], bb[:, c, 0:1], ALU.mult, ALU.add).then_inc(scans_done, 1)
                    v.wait_ge(ev_ready, b + 1)
                    for c in range(KD):
                        v.tensor_tensor_scan(aa[:, c, 1:BW + 1], keep[:, c, :], ev[:, c, :], aa[:, c, 0:1], ALU.mult, ALU.add).then_inc(scans_done, 1)

                def recurrence_3(b):
                    v.wait_ge(fraction_ready, 2 * b + 1)
                    v.wait_ge(copied, (b + 1) * NPROD)
                    chain.link(v.scalar_tensor_tensor(peak[:], kvr[:, R_, b % 2], 1.0, peak[:], ALU.add, ALU.mult))
                    chain.link(v.reciprocal(peak[:], peak[:]))
                    v.wait_ge(fraction_ready, 2 * b + 2)
                    if b >= 1:
                        v.wait_ge(out_ready, b * BT)
                    v.tensor_tensor(y[:], keep[:], peak[:], ALU.mult).then_inc(y_ready, 1)

                def add_out(b):
                    for t in range(b * BT, (b + 1) * BT):
                        v.wait_ge(out_ready, t + 1)
                        v.wait_ge(x_add_loaded[t % 2], 16 * (t // 2 + 1))
                        v.tensor_tensor(x_add[:, t % 2, :], p_out[:, t % 2, :], x_add[:, t % 2, :], ALU.add).then_inc(out_added, 1)

                front(0)
                v.wait_ge(w_exp, 1)
                chain.step(v.tensor_scalar(w[:], w[:], -1.0, None, ALU.mult))
                chain.step(v.tensor_scalar(mix1[:], mix[:], -1.0, 1.0, ALU.mult, ALU.add))
                chain.wait()
                finish_mix(0, K_)
                finish_mix(0, V_)
                for b in range(NB + 1):
                    if b < NB:
                        finish_mix(b, R_)
                    if b + 1 < NB:
                        front(b + 1)
                    if b >= 1:
                        recurrence_1(b - 1)
                    if b + 1 < NB:
                        finish_mix(b + 1, K_)
                    if b >= 1:
                        recurrence_2(b - 1)
                    if b + 1 < NB:
                        finish_mix(b + 1, V_)
                    if b >= 1:
                        recurrence_3(b - 1)
                        add_out(b - 1)

            @block.tensor
            def _(pe):
                def turn(b):
                    pe.wait_ge(normed, (b + 1) * BT)
                    for c in range(KD):
                        n = b * KD + c
                        if n >= 2:
                            pe.wait_ge(xT_ready, (n - 2) + (n - 2) // KD + 2)
                        for t in range(BT):
                            m = pe.transpose(p_turn[:, n % 2, t * P:(t + 1) * P], xn[:, t, c * P:(c + 1) * P], ident)
                        m.then_inc(turned, 1)

                def project(b, j):
                    pe.wait_ge(mixed_ready, (b * 3 + j + 1) * KD)
                    for c in range(KD):
                        n = b * NPROD + j * KD + c
                        if n >= 4:
                            pe.wait_ge(copied, n - 3)
                        for kc in range(KD):
                            m = pe.matmul(p_mm[:, n % 4, :], wkvr[:, j, kc, c * P:(c + 1) * P], mixed[:, (b * 3 + j) % NMIX, kc, :],
                                          start=(kc == 0), stop=(kc == KD - 1))
                        m.then_inc(product, 1)

                def output(b):
                    pe.wait_ge(y_ready, b + 1)
                    for i in range(BT):
                        t = b * BT + i
                        if t >= 2:
                            pe.wait_ge(out_added, t - 1)
                        for c in range(KD):
                            m = pe.matmul(p_out[:, t % 2, :], y[:, c, i * P:(i + 1) * P], wo[:, c, :], start=(c == 0), stop=(c == KD - 1))
                        m.then_inc(out_ready, 1)

                turn(0)
                pe.wait_ge(w_loaded, 16)
                pe.wait_ge(wo_loaded, 16)
                for b in range(NB):
                    project(b, K_)
                    if b + 1 < NB:
                        turn(b + 1)
                    project(b, V_)
                    project(b, R_)
                    if b >= 1:
                        output(b - 1)
                output(NB - 1)



def on_partitions(w):
    return np.ascontiguousarray(w.reshape(-1, P, w.shape[-1]).transpose(1, 0, 2))


def lay_ffn(inputs):
    a = {n: np.asarray(inputs["L0_ffn_" + n]) for n in ("gate_w", "w_gate", "w_up", "w_down", "sw_gate", "sw_up", "sw_down")}
    pair = np.stack([a["w_gate"], a["w_up"]], 2)
    pair = pair.reshape(E, KD, P, 2 * M).transpose(0, 2, 1, 3)
    shared = np.stack([a["sw_gate"], a["sw_up"]], 1)
    shared = shared.reshape(KD, P, 2, SM).transpose(1, 0, 2, 3)
    return {
        "gate_w": on_partitions(a["gate_w"]),
        "sup": np.ascontiguousarray(shared),
        "sdown": np.ascontiguousarray(a["sw_down"]),
        "upw": np.ascontiguousarray(pair.reshape(E, P, UP)),
        "downw": np.ascontiguousarray(a["w_down"]),
    }


def lay_rwkv(inputs):
    a = {n: np.asarray(inputs["L0_attn_b_" + n]) for n in
         ("time_decay", "time_first", "time_mix_k", "time_mix_v", "time_mix_r", "key_w", "value_w", "receptance_w", "output_w")}
    column = lambda v: v.reshape(KD, P).T
    return {
        "mixes": np.ascontiguousarray(np.stack([column(a["time_mix_" + n]) for n in "kvr"], 1)),
        "decay": np.ascontiguousarray(column(a["time_decay"])),
        "first": np.ascontiguousarray(column(a["time_first"])),
        "wkvr": np.ascontiguousarray(np.stack([on_partitions(a[n].T) for n in ("key_w", "value_w", "receptance_w")], 1)),
        "wout": on_partitions(a["output_w"].T),
    }


OPERANDS = ["x", "w_project", "w_attn_out", "gate_w", "shared_up", "shared_down", "expert_up", "expert_down",
            "mixes", "decay", "first", "w_kvr", "w_rwkv_out"]


def build(nc, x, w_project, w_attn_out, gate_w, shared_up, shared_down, expert_up, expert_down,
          mixes, decay, first, w_kvr, w_rwkv_out, out):
    x2, out2 = x.rearrange("b t d -> (b t) d"), out.rearrange("b t d -> (b t) d")
    with ExitStack() as ctx:
        k = Kernel(nc)
        qk_hi, qk_lo = k.dram("qk_hi", [2 * D, T]), k.dram("qk_lo", [2 * D, T])
        shift_rows = k.dram("shift_rows", [2, T])
        ident = ctx.enter_context(nc.sbuf_tensor("ident", [P, P], F32))[:]

        def layer(n, fill):
            xn_rows, acc_rows = k.dram(f"xn_rows{n}", [ROWS, D]), k.dram(f"acc_rows{n}", [ROWS, D])
            with ExitStack() as s:
                disp = Dispatch(k, s, f"disp{n}")
                with ExitStack() as r:
                    resid = r.enter_context(nc.sbuf_tensor(f"resid{n}", [P, NT, D], F32))
                    fill(resid)
                    stage_router(k, f"f{n}", ident, resid, gate_w, shared_up, shared_down, xn_rows, acc_rows, disp)
                    k.end_stage()
                stage_experts(k, f"g{n}", ident, expert_up, expert_down, xn_rows, acc_rows, disp)
                k.end_stage()
            return acc_rows[0:T, :]

        def attention(resid):
            with ExitStack() as s:
                values = s.enter_context(nc.sbuf_tensor("values", [P, NT, D], F32))
                stage_qkv(k, x2, w_project, ident, values, qk_hi, qk_lo)
                k.end_stage()
                heads = s.enter_context(nc.sbuf_tensor("heads", [P, NT, D], F32))
                stage_attention(k, ident, values, qk_hi, qk_lo, shift_rows, heads)
                k.end_stage()
                stage_attn_out(k, x2, w_attn_out, ident, heads, resid)
                k.end_stage()

        first_rows = layer(1, attention)
        time_mixed = k.dram("time_mixed", [T, D])
        stage_rwkv(k, ident, first_rows, mixes, decay, first, w_kvr, w_rwkv_out, time_mixed)
        k.end_stage()

        resid_loaded = k.sem("resid_loaded")

        def load(resid):
            with nc.Block() as block:
                @block.sync
                def _(sp):
                    sp.dma_start(resid[:], rows(time_mixed)).then_inc(resid_loaded, 16)
                    sp.wait_ge(resid_loaded, 16)

        second_rows = layer(2, load)
        out_stored = k.sem("out_stored")
        with nc.Block() as block:
            @block.sync
            def _(sp):
                sp.dma_start(out2, second_rows).then_inc(out_stored, 16)
                sp.wait_ge(out_stored, 16)


def kernel(**inputs):
    import concourse.bacc as bacc
    from concourse.bass_utils import run_bass_kernel_spmd

    ffn, rwkv = lay_ffn(inputs), lay_rwkv(inputs)
    x = np.ascontiguousarray(np.asarray(inputs["L0_attn_a_x"]))
    laid_out = {
        "x": x,
        "w_project": on_partitions(np.asarray(inputs["L0_attn_a_w_project"]).T),
        "w_attn_out": on_partitions(np.asarray(inputs["L0_attn_a_w_out"]).T),
        "gate_w": ffn["gate_w"], "shared_up": ffn["sup"], "shared_down": ffn["sdown"],
        "expert_up": ffn["upw"], "expert_down": ffn["downw"],
        "mixes": rwkv["mixes"], "decay": rwkv["decay"], "first": rwkv["first"],
        "w_kvr": rwkv["wkvr"], "w_rwkv_out": rwkv["wout"],
    }
    nc = bacc.Bacc("TRN2", target_bir_lowering=False, num_devices=1)
    arrays, args = {}, []
    for name in OPERANDS:
        arrays[f"in_{name}_dram"] = laid_out[name]
        args.append(nc.dram_tensor(f"in_{name}_dram", laid_out[name].shape, F32, kind="ExternalInput").ap())
    args.append(nc.dram_tensor("out_0_dram", x.shape, F32, kind="ExternalOutput").ap())
    build(nc, *args)
    result = run_bass_kernel_spmd(nc, [arrays], core_ids=[0])
    return result.results[0]["out_0_dram"]
```
